# Optimizing a Trainium2 kernel written in Bass

```python
import numpy as np
import jax
import jax.numpy as jnp

def _softmax(x, axis=-1):
    return jax.nn.softmax(x, axis=axis)

def _gelu(x):
    return jax.nn.gelu(x, approximate=True)

def _silu(x):
    return jax.nn.silu(x)

def _sigmoid(x):
    return jax.nn.sigmoid(x)

def _layernorm(x, axis=-1, eps=1e-05):
    m = jnp.mean(x, axis=axis, keepdims=True)
    v = jnp.var(x, axis=axis, keepdims=True)
    return (x - m) / jnp.sqrt(v + eps)

def _scatter_add(tgt, idx, src, axis=0):
    return tgt.at[idx].add(src)

def _segment_sum(src, seg, n):
    return jax.ops.segment_sum(src, seg, n)
kernel_name = 'mk_gnn_ffn_d1_gnn_r8_41906c'

def setup_inputs(seed: int=0):
    np.random.seed(seed)
    _w = jnp.asarray

    def _rec_inputs():
        import jax
        import jax.numpy as jnp
        _gk = jax.random.key(seed)
        x = -0.0003713 + 1 * jax.random.normal(jax.random.fold_in(_gk, 1), (6250, 256), jnp.float32)
        src = jax.random.randint(jax.random.fold_in(_gk, 2), (200000,), 0, 6250, jnp.int32)
        dst = jax.random.randint(jax.random.fold_in(_gk, 3), (200000,), 0, 6250, jnp.int32)
        _o = jnp.argsort(dst, stable=True)
        src = src[_o]
        dst = dst[_o]
        return (x, src, dst)
    x, src, dst = _rec_inputs()

    def _L0_gnn_setup():
        import jax, jax.numpy as jnp
        import numpy as np
        N = 6250
        E = 100000
        D_IN = 256
        D_H = 512
        D_OUT = 256
        key = jax.random.key(seed)
        ks = jax.random.split(key, 12)
        s = lambda d: 1.0 / np.sqrt(d)
        x = jax.random.normal(ks[0], (N, D_IN), dtype=jnp.float32)
        edge_index = jax.random.randint(ks[1], (2, E), 0, N, dtype=jnp.int64)
        W_rel = jax.random.uniform(ks[2], (D_IN, D_H), jnp.float32, -s(D_IN), s(D_IN))
        b_rel = jax.random.uniform(ks[3], (D_H,), jnp.float32, -s(D_IN), s(D_IN))
        W_root = jax.random.uniform(ks[4], (D_IN, D_H), jnp.float32, -s(D_IN), s(D_IN))
        W_ih = jax.random.uniform(ks[5], (4 * D_H, D_H), jnp.float32, -s(D_H), s(D_H))
        W_hh = jax.random.uniform(ks[6], (4 * D_H, D_H), jnp.float32, -s(D_H), s(D_H))
        b_ih = jax.random.uniform(ks[7], (4 * D_H,), jnp.float32, -s(D_H), s(D_H))
        b_hh = jax.random.uniform(ks[8], (4 * D_H,), jnp.float32, -s(D_H), s(D_H))
        W_fc = jax.random.uniform(ks[9], (D_H, D_OUT), jnp.float32, -s(D_H), s(D_H))
        b_fc = jax.random.uniform(ks[10], (D_OUT,), jnp.float32, -s(D_H), s(D_H))
        return {'x': x, 'edge_index': edge_index, 'W_rel': W_rel, 'b_rel': b_rel, 'W_root': W_root, 'W_ih': W_ih, 'W_hh': W_hh, 'b_ih': b_ih, 'b_hh': b_hh, 'W_fc': W_fc, 'b_fc': b_fc}
    _L0_gnn_all = _L0_gnn_setup()
    _L0_gnn_in = {k: v for k, v in _L0_gnn_all.items() if k in ('W_rel', 'b_rel', 'W_root', 'W_ih', 'W_hh', 'b_ih', 'b_hh', 'W_fc', 'b_fc')}
    del _L0_gnn_all

    def _L0_ffn_setup():
        import math
        import jax, jax.numpy as jnp
        import numpy as np
        CAPACITY_FACTOR = 1.25
        key = jax.random.key(seed)
        ks = jax.random.split(key, 5)
        B, L, D, F, E = (8, 1024, 256, 1024, 8)
        h = jax.random.normal(ks[0], (B, L, D), dtype=jnp.float32)
        gate_w = jax.random.normal(ks[1], (D, E), dtype=jnp.float32) * 0.02
        gate_b = jnp.zeros((E,), dtype=jnp.float32)
        w1 = jax.random.normal(ks[2], (E, D, F), dtype=jnp.float32) * (1.0 / math.sqrt(D))
        b1 = jnp.zeros((E, F), dtype=jnp.float32)
        w2 = jax.random.normal(ks[3], (E, F, D), dtype=jnp.float32) * (1.0 / math.sqrt(F))
        b2 = jnp.zeros((E, D), dtype=jnp.float32)
        return {'h': h, 'gate_w': gate_w, 'gate_b': gate_b, 'w1': w1, 'b1': b1, 'w2': w2, 'b2': b2}
    _L0_ffn_all = _L0_ffn_setup()
    _L0_ffn_in = {k: v for k, v in _L0_ffn_all.items() if k in ('gate_w', 'gate_b', 'w1', 'b1', 'w2', 'b2')}
    del _L0_ffn_all
    return {'x': x, 'src': src, 'dst': dst, 'L0_gnn_W_rel': _L0_gnn_in['W_rel'], 'L0_gnn_b_rel': _L0_gnn_in['b_rel'], 'L0_gnn_W_root': _L0_gnn_in['W_root'], 'L0_gnn_W_ih': _L0_gnn_in['W_ih'], 'L0_gnn_W_hh': _L0_gnn_in['W_hh'], 'L0_gnn_b_ih': _L0_gnn_in['b_ih'], 'L0_gnn_b_hh': _L0_gnn_in['b_hh'], 'L0_gnn_W_fc': _L0_gnn_in['W_fc'], 'L0_gnn_b_fc': _L0_gnn_in['b_fc'], 'L0_ffn_gate_w': _L0_ffn_in['gate_w'], 'L0_ffn_gate_b': _L0_ffn_in['gate_b'], 'L0_ffn_w1': _L0_ffn_in['w1'], 'L0_ffn_b1': _L0_ffn_in['b1'], 'L0_ffn_w2': _L0_ffn_in['w2'], 'L0_ffn_b2': _L0_ffn_in['b2']}

def reference(x, src, dst, L0_gnn_W_rel, L0_gnn_b_rel, L0_gnn_W_root, L0_gnn_W_ih, L0_gnn_W_hh, L0_gnn_b_ih, L0_gnn_b_hh, L0_gnn_W_fc, L0_gnn_b_fc, L0_ffn_gate_w, L0_ffn_gate_b, L0_ffn_w1, L0_ffn_b1, L0_ffn_w2, L0_ffn_b2):
    import jax
    import jax.numpy as jnp

    def _L0_gnn_ref(x, edge_index, W_rel, b_rel, W_root, W_ih, W_hh, b_ih, b_hh, W_fc, b_fc):
        import jax, jax.numpy as jnp
        import numpy as np
        N = 6250
        E = 100000
        D_IN = 256
        D_H = 512
        D_OUT = 256
        src, dst = (edge_index[0], edge_index[1])
        agg = jax.ops.segment_sum(x[src], dst, num_segments=N)
        h = jax.nn.relu(agg @ W_rel + b_rel + x @ W_root)
        gates = h @ W_ih.T + b_ih + b_hh
        i, f, g, o = jnp.split(gates, 4, axis=-1)
        c = jax.nn.sigmoid(i) * jnp.tanh(g)
        h_lstm = jax.nn.sigmoid(o) * jnp.tanh(c)
        return h_lstm @ W_fc + b_fc

    def _L0_ffn_ref(h, gate_w, gate_b, w1, b1, w2, b2):
        import math
        import jax, jax.numpy as jnp
        import numpy as np
        CAPACITY_FACTOR = 1.25
        B, L, D = h.shape
        E = gate_w.shape[1]
        T = B * L
        C = max(1, math.ceil(CAPACITY_FACTOR * T / E))
        x = h.reshape(T, D)
        logits = x @ gate_w + gate_b
        probs = jax.nn.softmax(logits, axis=-1)
        idx = jnp.argmax(probs, axis=-1)
        prb = jnp.take_along_axis(probs, idx[:, None], axis=1)[:, 0]
        one_hot = jax.nn.one_hot(idx, E, dtype=jnp.float32)
        pos = (jnp.cumsum(one_hot, axis=0) * one_hot).sum(-1).astype(jnp.int32) - 1
        kept = pos < C
        pos_safe = jnp.where(kept, pos, C)
        buf = jnp.zeros((E, C, D), dtype=h.dtype).at[idx, pos_safe].set(x, mode='drop')
        hmid = jax.nn.relu(jnp.einsum('ecd,edf->ecf', buf, w1) + b1[:, None, :])
        ybuf = jnp.einsum('ecf,efd->ecd', hmid, w2) + b2[:, None, :]
        pos_g = jnp.minimum(pos, C - 1)
        y_tok = ybuf[idx, pos_g] * (prb * kept)[:, None]
        y = y_tok.reshape(B, L, D)
        y = jnp.nan_to_num(y, nan=0.0, posinf=10000.0, neginf=-10000.0)
        return y
    edge_index = jnp.stack([src, dst])
    x = x + _L0_gnn_ref(_layernorm(x, axis=-1), edge_index, L0_gnn_W_rel, L0_gnn_b_rel, L0_gnn_W_root, L0_gnn_W_ih, L0_gnn_W_hh, L0_gnn_b_ih, L0_gnn_b_hh, L0_gnn_W_fc, L0_gnn_b_fc)
    x = x + _L0_ffn_ref(_layernorm(x, axis=-1)[None], L0_ffn_gate_w, L0_ffn_gate_b, L0_ffn_w1, L0_ffn_b1, L0_ffn_w2, L0_ffn_b2)[0]
    return x

_drawn_inputs = setup_inputs


def setup_inputs(seed=0):
    import zlib

    import numpy as np

    out = dict(_drawn_inputs(seed))
    spreads = {'L0_ffn_gate_b': (0.0, 0.1), 'L0_ffn_b1': (0.0, 0.609), 'L0_ffn_b2': (0.0, 0.43)}
    factors = {'L0_gnn_b_rel': 8.0, 'L0_gnn_b_ih': 8.0, 'L0_gnn_b_hh': 8.0}
    for name, (base, spread) in spreads.items():
        noise = np.random.default_rng([zlib.crc32(name.encode()), seed]).standard_normal(out[name].shape)
        drawn = base * np.exp(spread * noise) if base else spread * noise
        out[name] = jnp.asarray(drawn.astype(out[name].dtype))
    for name, factor in factors.items():
        out[name] = (out[name] * factor).astype(out[name].dtype)
    return out
```

```python
from contextlib import ExitStack

import concourse.bass as bass
from concourse import mybir

ALU = mybir.AluOpType
ACT = mybir.ActivationFunctionType
AX = mybir.AxisListType.X
F32 = mybir.dt.float32
F32R = mybir.dt.float32r
BF16 = mybir.dt.bfloat16
I32 = mybir.dt.int32
U16 = mybir.dt.uint16
U8 = mybir.dt.uint8
ds = bass.ds

P = 128
N, D = 6250, 256
E = 200000
H = 512
NEXP, F = 8, 1024
CAP = -(-5 * N // (4 * NEXP))
EPS = 1e-5
BIG = 3.4028235e38

GT = 4
NG = -(-E // (P * GT))
TR = 13
NT = TR * P
GPAD = NT // GT
RING = 8
BLK = 50
CH = 2
NCH = BLK // CH
CT = CH * P
FULL = N // P
REST = N - FULL * P
PADDST = N + 10
SLOTS = 1024
ROW = 528
RES, LOG, TOK = D, 2 * D, 2 * D + NEXP
NSLOT = NEXP * SLOTS
NOSLOT = 9000
HALF = (512, CAP - 512 + (CAP & 1))


def build(nc, x, src, dst, W_rel, b_rel, W_root, W_ih, W_hh, b_ih, b_hh, W_fc, b_fc,
          gate_w, gate_b, w1, b1, w2, b2, out):
    xn_tab = nc.dram_tensor("xn_tab", (BLK * P, D), F32).ap()
    x_pad = nc.dram_tensor("x_pad", (BLK * P, D), F32).ap()
    slots = nc.dram_tensor("slots", (NSLOT, ROW), F32).ap()
    gtab = nc.dram_tensor("gtab", (2, TR, P // GT), I32).ap()

    with ExitStack() as ctx:
        def sb(name, shape, dt):
            return ctx.enter_context(nc.sbuf_tensor(name, shape, dt))

        def sem(name):
            return ctx.enter_context(nc.semaphore(name))

        agg = sb("agg", [P, BLK, D], F32)
        aggf = agg[:, :, :].rearrange("p b d -> p (b d)")
        ring = sb("ring", [P, RING, GT, D], F32)
        ringf = ring[:, :, :, :].rearrange("p r t d -> p (r t d)")
        ringi = ringf.bitcast(I32)
        srcT = sb("srcT", [P, NG * GT], U16)
        dstT = sb("dstT", [P, NG * GT], U16)
        ids = sb("ids", [P, RING * GT], I32)
        plan = sb("plan", [1, GPAD], I32)
        ident = sb("ident", [P, P], F32)
        iota_d = sb("iota_d", [P, P], F32)
        tri = sb("tri", [P, P], BF16)
        ones = sb("ones", [P, P], BF16)
        blk_base = sb("blk_base", [P, BLK], F32)
        tok_code = sb("tok_code", [P, BLK], F32)
        valid = sb("valid", [P, BLK], F32)
        e_base = sb("e_base", [P, CH, NEXP], F32)
        e_rank = sb("e_rank", [P, CH, NEXP], F32)
        Wrr = [sb(f"Wrr_{q}", [P, 4, H], F32R) for q in ("hi", "lo")]
        Wg = [sb(f"Wg_{q}", [P, 4, 3 * H], F32R) for q in ("hi", "lo")]
        Wfc = [sb(f"Wfc_{q}", [P, 4, D], F32R) for q in ("hi", "lo")]
        xa = [sb(f"xa_{q}", [P, 4, CT], F32R) for q in ("hi", "lo")]
        hT = [sb(f"hT_{q}", [P, 4, CT], F32R) for q in ("hi", "lo")]
        bias = sb("bias", [P, 100], F32)
        gbias = sb("gbias", [P, 16], F32)
        b1c = sb("b1c", [P, 2, 8], F32)
        bfc = sb("bfc", [P, 1, D], F32)
        gw = sb("gw", [P, 2, NEXP], F32)
        gb = sb("gb", [P, CH, NEXP], F32)
        S = sb("S", [P, GT, P], F32)
        rel = sb("rel", [P, GT], F32)
        wk = sb("wk", [P, 5664], F32)
        sm = sb("sm", [P, 240], F32)
        carry = sb("carry", [P, NEXP], F32)
        idx = sb("idx", [P, CH], I32)
        epst = sb("epst", [P, 1], F32)

        def cut(t, at, *shape):
            n = 1
            for s in shape:
                n *= s
            v = t[:, at:at + n]
            if len(shape) == 2:
                v = v.rearrange("p (a b) -> p a b", a=shape[0])
            if len(shape) == 3:
                v = v.rearrange("p (a b c) -> p a b c", a=shape[0], b=shape[1])
            return v

        agg_blk = cut(wk, 0, CH, D)
        xn_rows = cut(wk, 512, CH, D)
        x_rows = cut(wk, 1024, CH, D)
        hf = cut(wk, 1536, 4, CT)
        sg = cut(wk, 2560, 2, 3, CT)
        x2nT = cut(wk, 4096, 2, CT)
        pay = cut(wk, 4608, CH, ROW)
        stats = cut(sm, 0, CH, 6)
        mv = cut(sm, 12, CH, 2)
        rstd = cut(sm, 16, CH)
        lg = cut(sm, 24, CH, NEXP)
        mx = cut(sm, 40, CH)
        sc = cut(sm, 48, CH, NEXP)
        m2 = cut(sm, 64, CH)
        pin = cut(sm, 72, CH, NEXP)
        pw = cut(sm, 88, CH, NEXP)
        pp = cut(sm, 104, CH, NEXP)
        wsum = cut(sm, 120, CH)
        psum_ = cut(sm, 122, CH)
        kept = cut(sm, 124, CH)
        kept2 = cut(sm, 126, CH)
        slotf = cut(sm, 128, CH)
        ln_stats = cut(sm, 136, 8, 6)
        ln_mv = cut(sm, 184, 8, 2)
        ln_rstd = cut(sm, 200, 8)
        oh = sb("oh", [P, CH, NEXP], BF16)

        w_stage = wk[:, 0:5120]
        ed = [ringi[:, 0:NT], ringi[:, NT:2 * NT]]
        edf = [ringf[:, 0:NT], ringf[:, NT:2 * NT]]
        kmm = cut(ringf, 2 * NT, 2, TR)
        gmm = cut(ringi, 2 * NT + 32, 2, P // GT)
        b_stage = ringf[:, 7040:7168]
        PR = 3456

        def prow(k, pad=0, n=GPAD):
            a = PR + k * 448 + pad
            return ringi[0:1, a:a + n]

        rows = [cut(aggf, h * 4 * ROW, 4, ROW) for h in range(2)]
        w1s = aggf[:, 4224:6272]
        w2s = aggf[:, 6272:8320]
        b2t = [aggf[:, 8320 + D * q:8320 + D * (q + 1)] for q in range(2)]
        U0 = 8832

        def ut(k):
            return cut(aggf, U0 + 512 * k, 2, D)

        yb = ut(0)
        qv = [ut(1), ut(2)]
        rr = [ut(3), ut(4)]
        g2 = ut(5)
        ov = [ut(6), cut(wk, 4608, 2, D)]
        fin_mask = sb("fin_mask", [P, 2, D], U8)
        es = cut(sm, 24, 4, NEXP)
        ssum = cut(sm, 64, 4)
        rp = cut(sm, 72, 4)
        tokf = cut(sm, 80, 4)
        tok_i = sb("tok_i", [P, 4], I32)
        wbuf1 = [[Wg[q][:, :, :].rearrange("p a b -> p (a b)")[:, 2048 * k:2048 * (k + 1)] for q in range(2)]
                 for k in range(2)]
        wbuf2 = [[Wg[q][:, :, :].rearrange("p a b -> p (a b)")[:, 4096:6144] for q in range(2)],
                 [Wrr[q][:, :, :].rearrange("p a b -> p (a b)") for q in range(2)]]
        xT = [xa[q][:, :, :].rearrange("p a b -> p (a b)").rearrange("p (k n) -> p k n", k=2) for q in range(2)]
        hE = [hT[q][:, :, :].rearrange("p a b -> p (a b)").rearrange("p (k n) -> p k n", k=2) for q in range(2)]
        hfE = hf.rearrange("p a b -> p (a b)").rearrange("p (k n) -> p k n", k=2)

        ps = ctx.enter_context(nc.psum_tensor("ps", [P, 8, 512], F32))
        tr = [ps[:, 2, :], ps[:, 3, :]]
        tr2 = [t.rearrange("p (a b) -> p a b", a=2) for t in tr]

        pad_set, edges_in, edges_f, kmm_done, dstT_done = (sem(n) for n in (
            "pad_set", "edges_in", "edges_f", "kmm_done", "dstT_done"))
        x_in = [sem(f"x_in{i}") for i in range(7)]
        ln_done, ln_aggr, ln_sqrt, ln_chain = sem("ln_done"), sem("ln_aggr"), sem("ln_sqrt"), sem("ln_chain")
        consts, zero_set, x_copied, xn_out, table_zero = (sem(n) for n in (
            "consts", "zero_set", "x_copied", "xn_out", "table_zero"))
        et_made, et_read = sem("et_made"), sem("et_read")
        g_reduced, g_out, g_back, plan_chain, plan_done = (sem(n) for n in (
            "g_reduced", "g_out", "g_back", "plan_chain", "plan_done"))
        w_in, w_free, w_hi, w_lo, bias_in, bias_T, bias_done, small_in = (sem(n) for n in (
            "w_in", "w_free", "w_hi", "w_lo", "bias_in", "bias_T", "bias_done", "small_in"))
        wt_made, wt_hi, wt_lo = sem("wt_made"), sem("wt_hi"), sem("wt_lo")
        agg_zero, start_marks, carry_zero = sem("agg_zero"), sem("start_marks"), sem("carry_zero")
        ids_set = sem("ids_set")
        gath = [sem(f"gath{q}") for q in range(RING)]
        ring_ready, group_done = sem("ring_ready"), sem("group_done")
        rel_made = sem("rel_made")
        S_made = [sem(f"S_made{t}") for t in range(GT)]
        S_used = [sem(f"S_used{t}") for t in range(GT)]
        evac = sem("evac")
        blk_copied, xn_in, xr_in, trA, trX, xa_hi, xa_lo = (sem(n) for n in (
            "blk_copied", "xn_in", "xr_in", "trA", "trX", "xa_hi", "xa_lo"))
        fill_made, fill_read = sem("fill_made"), sem("fill_read")
        h_relu, h_hi, h_lo, gate_act, c_made, c_tanh, hl_made, hl_hi, hl_lo = (sem(n) for n in (
            "h_relu", "h_hi", "h_lo", "gate_act", "c_made", "c_tanh", "hl_made", "hl_hi", "hl_lo"))
        xb_made, x2_made, var_made, std_made, x2n_made, x2T_made, x2T_copied = (sem(n) for n in (
            "xb_made", "x2_made", "var_made", "std_made", "x2n_made", "x2T_made", "x2T_copied"))
        logit_made, oh_made, cum_made, route, pay_ready, scattered, x2_stored = (sem(n) for n in (
            "logit_made", "oh_made", "cum_made", "route", "pay_ready", "scattered", "x2_stored"))
        stage_in, stage_hi, stage_lo, b2_in = sem("stage_in"), sem("stage_hi"), sem("stage_lo"), sem("b2_in")
        rows_in = [sem(f"rows_in{h}") for h in range(2)]
        rows_T, ex_hi, ex_lo, mm1_made, e_relu, e_hi, e_lo, h_used = (sem(n) for n in (
            "rows_T", "ex_hi", "ex_lo", "mm1_made", "e_relu", "e_hi", "e_lo", "h_used"))
        y_made, y_read, exp_made, weight_chain, q_made, r_made, o_made, unit_chain, tok_made = (sem(n) for n in (
            "y_made", "y_read", "exp_made", "weight_chain", "q_made", "r_made", "o_made", "unit_chain", "tok_made"))
        out_scattered = [sem(f"out_scattered{u}") for u in range(2)]
        experts_start, b1_set, q_seen, idx_seen, o_seen = sem("experts_start"), sem("o_seen"), sem("idx_seen"), sem("b1_set"), sem("q_seen")
        ln_recip, kmmT, out_chain = sem("ln_recip"), sem("kmmT"), sem("out_chain")
        w_in2, w_in3 = sem("w_in2"), sem("w_in3")

        O_INIT, Y_INIT = 4, 2
        FILLS = 9
        ROUTE = 15

        def held(eng, reg, value, least, most):
            eng.reg_mov(reg, value)
            return eng.snap(reg, min_val=least, max_val=most)

        block = ctx.enter_context(nc.Block())

        @block.sync
        def _(sp):
            ed3 = [v.rearrange("p (q e) -> p q e", q=TR) for v in ed]
            whole = (TR - 1) * P
            more = E // P - whole
            sp.wait_ge(pad_set, 2)
            for v, a in ((ed3[0], dst), (ed3[1], src)):
                sp.dma_start(v[:, 0:TR - 1, :], a[0:whole * P].rearrange("(q r e) -> r q e", r=P, e=P)).then_inc(edges_in, 16)
                sp.dma_start(v[0:more, TR - 1, :], a[whole * P:(whole + more) * P].rearrange("(r e) -> r e", e=P)).then_inc(edges_in, 16)
                sp.dma_start(v[more:more + 1, TR - 1, 0:E % P], a[(whole + more) * P:E].rearrange("(r e) -> r e", r=1)).then_inc(edges_in, 16)
            for i in range(6):
                sp.dma_start(agg[:, 8 * i:8 * i + 8, :], x[1024 * i:1024 * (i + 1), :].rearrange("(b p) d -> p b d", p=P)).then_inc(x_in[i], 16)
            sp.dma_start(agg[0:REST, FULL, :], x[FULL * P:N, :]).then_inc(x_in[6], 16)
            sp.dma_start(cut(wk, 0, 2, H), W_rel.rearrange("(k p) n -> p k n", p=P)).then_inc(w_in, 16)
            sp.dma_start(cut(wk, 1024, 2, H), W_root.rearrange("(k p) n -> p k n", p=P)).then_inc(w_in, 16)
            sp.dma_start(cut(wk, 2048, 4, D), W_fc.rearrange("(k p) n -> p k n", p=P)).then_inc(w_in, 16)
            sp.dma_start(b_stage[0:4, :], b_rel.rearrange("(r p) -> r p", p=P)).then_inc(bias_in, 16)
            sp.dma_start(b_stage[4:20, :], b_ih.rearrange("(r p) -> r p", p=P)).then_inc(bias_in, 16)
            sp.dma_start(b_stage[20:36, :], b_hh.rearrange("(r p) -> r p", p=P)).then_inc(bias_in, 16)
            sp.dma_start(b_stage[36:100, :], b1.rearrange("e (r p) -> (e r) p", p=P)).then_inc(bias_in, 16)
            sp.dma_start(cut(wk, 3072, 4, H), W_ih[0:H, :].rearrange("(r p) n -> p r n", p=P)).then_inc(w_in, 16)
            sp.dma_start(bfc[:, 0, :], b_fc.rearrange("(a d) -> a d", a=1).to_broadcast([P, D])).then_inc(small_in, 16)
            for c in range(CH):
                sp.dma_start(gb[:, c, :], gate_b.rearrange("(a d) -> a d", a=1).to_broadcast([P, NEXP])).then_inc(small_in, 16)
            sp.dma_start(gw[:, :, :], gate_w.rearrange("(k p) e -> p k e", p=P)).then_inc(small_in, 16)
            sp.wait_ge(g_reduced, 2)
            for m in range(2):
                sp.dma_start(gtab[m], gmm[0:TR, m, :]).then_inc(g_out, 16)
            sp.wait_ge(g_out, 32)
            sp.dma_start(ringi[0:1, PR:PR + GPAD], gtab[0].rearrange("r g -> (r g)").rearrange("(a n) -> a n", a=1)).then_inc(g_back, 16)
            sp.dma_start(ringi[0:1, PR + 448:PR + 448 + GPAD], gtab[1].rearrange("r g -> (r g)").rearrange("(a n) -> a n", a=1)).then_inc(g_back, 16)
            sp.wait_ge(w_lo, 3)
            sp.dma_start(cut(wk, 0, 4, H), W_ih[2 * H:3 * H, :].rearrange("(r p) n -> p r n", p=P)).then_inc(w_in2, 16)
            sp.wait_ge(wt_made, 4)
            sp.dma_start(cut(wk, 3072, 4, H), W_ih[3 * H:4 * H, :].rearrange("(r p) n -> p r n", p=P)).then_inc(w_in3, 16)
            for i in range(6):
                sp.wait_ge(ln_done, 8 * (i + 1))
                sp.dma_start(xn_tab[1024 * i:1024 * (i + 1), :].rearrange("(b p) d -> p b d", p=P), agg[:, 8 * i:8 * i + 8, :]).then_inc(xn_out, 16)
            sp.wait_ge(ln_done, FULL + 1)
            sp.dma_start(xn_tab[FULL * P:N, :], agg[0:REST, FULL, :]).then_inc(xn_out, 16)
            sp.dma_start(x_pad[0:N, :], x[:, :]).then_inc(x_copied, 16)
            sp.wait_ge(zero_set, 1)
            z = wk[:, 4608:4608 + 512]
            zr = (BLK * P - N) * D // 512
            for t in (xn_tab, x_pad):
                sp.dma_start(t[N:BLK * P, :].rearrange("(p r) d -> p (r d)", r=2), z[0:zr, :]).then_inc(xn_out, 16)
            zrow = wk[:, 4608:4608 + CH * ROW]
            for q in range(8):
                sp.dma_start(slots[q * 1024:(q + 1) * 1024, :].rearrange("(p a r) w -> p a (r w)", p=P, r=CH),
                             zrow.rearrange("p (o w) -> p o w", o=1).to_broadcast([P, 4, CH * ROW])).then_inc(table_zero, 16)
            sp.wait_ge(x_copied, 16)
            sp.wait_ge(xn_out, 9 * 16)

            def load_rows(c):
                sp.dma_start(xn_rows, xn_tab[ds(c * CT, CT), :].rearrange("(b p) d -> p b d", p=P)).then_inc(xn_in, 16)
                sp.dma_start(x_rows, x_pad[ds(c * CT, CT), :].rearrange("(b p) d -> p b d", p=P)).then_inc(xr_in, 16)

            load_rows(0)
            with sp.Fori(0, NCH - 1) as c:
                sp.wait_ge(x2_made, c + 1)
                load_rows(c + 1)
                sp.dma_start(out[ds(c * CT, CT), :].rearrange("(b p) d -> p b d", p=P), pay[:, :, RES:RES + D]).then_inc(x2_stored, 16)
            sp.wait_ge(x2_made, NCH)
            sp.dma_start(out[FULL * P:N, :], pay[0:REST, 0, RES:RES + D]).then_inc(x2_stored, 16)

            sp.wait_ge(experts_start, 1)
            sp.wait_ge(x2_stored, 16 * (NCH + 1))
            sp.wait_ge(scattered, 16 * CH * (NCH + 1))
            with sp.Fori(0, NEXP // 2) as ep:
                for q in range(2):
                    e = ep * 2 + q
                    sp.wait_ge(stage_lo, e * 2 + 1)
                    sp.dma_start(w1s.rearrange("p (k n) -> p k n", k=2), w1[ds(e, 1)].rearrange("o (k p) n -> p (o k) n", p=P)).then_inc(stage_in, 16)
                    sp.dma_start(w2s.rearrange("p (k n) -> p k n", k=8), w2[ds(e, 1)].rearrange("o (k p) n -> p (o k) n", p=P)).then_inc(stage_in, 16)
                    for h in range(2):
                        sp.wait_ge(o_made, O_INIT + e * 4 + 2 * h - 2)
                        if h == 0:
                            sp.dma_start(b2t[q], b2[ds(e, 1), :].to_broadcast([P, D])).then_inc(b2_in, 16)
                        sp.dma_start(rows[h], slots[ds(e * SLOTS + h * 512, 512), :].rearrange("(t p) w -> p t w", p=P)).then_inc(rows_in[h], 16)

        @block.gpsimd
        def _(pool):
            g = nc.gpsimd
            g.memset(ident[:, :], 0.0).then_inc(consts, 1)
            g.memset(tri[:, :], 1.0).then_inc(consts, 1)
            g.memset(ones[:, :], 1.0).then_inc(consts, 1)
            pool.wait_ge(consts, 2)
            g.affine_select(out=ident[:, :], in_=ident[:, :], compare_op=ALU.not_equal, fill=1.0, base=0,
                            pattern=[[-1, P]], channel_multiplier=1).then_inc(consts, 1)
            g.affine_select(out=tri[:, :], in_=tri[:, :], compare_op=ALU.is_ge, fill=0.0, base=0,
                            pattern=[[1, P]], channel_multiplier=-1).then_inc(consts, 1)
            fl = dict(allow_small_or_imprecise_dtypes=True)
            g.iota(iota_d[:, :], pattern=[[1, P]], base=0, channel_multiplier=0, **fl).then_inc(consts, 1)
            g.iota(blk_base[:, :], pattern=[[P, BLK]], base=0, channel_multiplier=0, **fl).then_inc(consts, 1)
            g.iota(tok_code[:, :], pattern=[[P, BLK]], base=-NSLOT, channel_multiplier=1, **fl).then_inc(consts, 1)
            g.iota(e_base[:, :, :], pattern=[[0, CH], [SLOTS, NEXP]], base=0, channel_multiplier=0, **fl).then_inc(consts, 1)
            g.iota(e_rank[:, :, :], pattern=[[0, CH], [-1, NEXP]], base=NEXP, channel_multiplier=0, **fl).then_inc(consts, 1)
            g.memset(idx[:, :], NOSLOT).then_inc(consts, 1)
            g.iota(prow(4), pattern=[[1, GPAD]], base=0, channel_multiplier=0).then_inc(consts, 1)
            for n, (hi, lo, a, b) in enumerate((
                    (Wrr[0][:, 0:2, :], Wrr[1][:, 0:2, :], 0, 1024), (Wrr[0][:, 2:4, :], Wrr[1][:, 2:4, :], 1024, 2048),
                    (Wfc[0][:, :, :], Wfc[1][:, :, :], 2048, 3072))):
                pool.wait_ge(w_hi, n + 1)
                g.tensor_tensor(lo.rearrange("p a b -> p (a b)"), wk[:, a:b],
                                hi.rearrange("p a b -> p (a b)").bitcast(F32), ALU.subtract).then_inc(w_lo, 1)

            pool.wait_ge(xn_out, 9 * 16)
            pool.wait_ge(et_read, 8)
            pool.wait_ge(plan_done, 1)
            cc = pool.alloc_register("pool_chunk")
            pool.reg_mov(cc, 0)
            r_c = pool.alloc_register("pool_c")
            pool.wait_ge(table_zero, 8 * 16)
            marks = [pool.alloc_register(f"pool_mark{q}") for q in range(RING)]

            def scatter(c):
                pool.wait_ge(pay_ready, c + 1)
                pool.sem_inc(idx_seen, 1)
                for b in range(CH):
                    g.indirect_dma_start(out=slots, out_offset=bass.IndirectOffsetOnAxis(ap=idx[:, b:b + 1], axis=0),
                                         in_=pay[:, b, :], in_offset=None, bounds_check=NSLOT - 1, oob_is_err=False).then_inc(scattered, 16)

            HG = RING // 2

            def set_ids(i, q, count):
                g.tensor_copy(ids[:, q * GT:(q + count) * GT],
                              srcT[:, ds((i * RING + q) * GT, count * GT)]).then_inc(ids_set, 1)

            def groups(i, count, first=False, last=False):
                pool.load(marks[0:count], plan[0:1, ds(i * RING, count)])
                for q in range(count):
                    if q % HG == 0:
                        pool.wait_ge(ids_set, 2 * i + 1 + q // HG)
                    if not first:
                        pool.wait_ge(group_done, i * RING + q - RING + 1)
                    if q >= 2 or not first:
                        pool.wait_ge(gath[(q - 2) % RING], (i + (1 if q >= 2 else 0)) * 16 * GT)
                        pool.sem_inc(ring_ready, 1)
                    if q == 1:
                        set_ids(i, HG, count - HG)
                    if q == HG + 1 and not last:
                        set_ids(i + 1, 0, HG)
                    for t in range(GT):
                        g.indirect_dma_start(out=ring[:, q, t, :], out_offset=None, in_=xn_tab,
                                             in_offset=bass.IndirectOffsetOnAxis(ap=ids[:, q * GT + t:q * GT + t + 1], axis=0),
                                             bounds_check=BLK * P - 1, oob_is_err=False).then_inc(gath[q], 16)
                    flag = pool.snap(marks[q], min_val=0, max_val=(1 << 17) - 1)
                    with pool.If(flag >= (1 << 16)):
                        c = held(pool, r_c, cc, 0, NCH - 1)
                        scatter(c)
                        pool.reg_mov(cc, c + 1)

            set_ids(0, 0, HG)
            groups(0, RING, first=True)
            with pool.Fori(1, NG // RING) as i:
                groups(i, RING)
            groups(NG // RING, NG % RING, last=True)
            for q in (NG % RING - 2, NG % RING - 1):
                pool.wait_ge(gath[q], 16 * GT * (NG // RING + 1))
                pool.sem_inc(ring_ready, 1)
            c0 = pool.snap(cc, min_val=0, max_val=NCH - 1)
            with pool.Fori(c0, NCH) as c:
                scatter(c)
            scatter(NCH)

            def w_lo_parts(e, q):
                for n, (s, wb) in enumerate(((w1s, wbuf1[q]), (w2s, wbuf2[q]))):
                    pool.wait_ge(stage_hi, e * 2 + n + 1)
                    g.tensor_tensor(wb[1], s, wb[0].bitcast(F32), ALU.subtract).then_inc(stage_lo, 1)

            def out_rows(e, h, u):
                un = e * 4 + h * 2 + u
                pool.wait_ge(r_made, un + 1)
                pool.wait_ge(q_made, un + 2)
                pool.sem_inc(q_seen, 1)
                g.tensor_scalar(g2, qv[u], 0.0, 1e4, ALU.is_lt, ALU.mult).then_inc(unit_chain, 1)
                g.tensor_scalar(rr[u], qv[u], 0.0, 1e4, ALU.is_gt, ALU.mult).then_inc(unit_chain, 1)
                pool.wait_ge(unit_chain, un * 2 + 2)
                g.tensor_tensor(rr[u], rr[u], g2, ALU.subtract).then_inc(r_made, 1)

            def out_scatter(e, h, u):
                un = e * 4 + h * 2 + u
                pool.wait_ge(o_made, O_INIT + un + 1)
                pool.sem_inc(o_seen, 1)
                scatter_unit(u)

            def scatter_unit(u):
                for t in range(2):
                    g.indirect_dma_start(out=out, out_offset=bass.IndirectOffsetOnAxis(ap=tok_i[:, 2 * u + t:2 * u + t + 1], axis=0),
                                         in_=ov[u][:, t, :], in_offset=None, bounds_check=N - 1, oob_is_err=False).then_inc(out_scattered[u], 16)

            pool.wait_ge(experts_start, 1)
            pool.wait_ge(tok_made, 1)
            for u in range(2):
                scatter_unit(u)
            w_lo_parts(0, 0)
            with pool.Fori(0, NEXP // 2) as ep:
                for q in range(2):
                    e = ep * 2 + q
                    for h in range(2):
                        for u in range(2):
                            out_rows(e, h, u)
                        for u in range(2):
                            out_scatter(e, h, u)
                        if h == 0 and q == 0:
                            w_lo_parts(e + 1, 1)
                        if h == 0 and q == 1:
                            with pool.If(ep < NEXP // 2 - 1):
                                w_lo_parts(e + 1, 0)
            for u in range(2):
                pool.wait_ge(out_scattered[u], 32 * (2 * NEXP + 1))

        @block.scalar
        def _(act):
            a = nc.scalar
            for i in range(7):
                act.wait_ge(ln_aggr, i + 1)
                act.wait_ge(start_marks, 1)
                nb = 8 if i < 6 else 1
                n = P if i < 6 else REST
                a.activation(ln_rstd[0:n, 0:nb], ln_mv[0:n, 0:nb, 1], ACT.Sqrt, bias=epst[0:n, :]).then_inc(ln_sqrt, 1)
            for n, (hi, x0, x1) in enumerate(((Wrr[0][:, 0:2, :], 0, 1024), (Wrr[0][:, 2:4, :], 1024, 2048), (Wfc[0][:, :, :], 2048, 3072))):
                act.wait_ge(w_in, 64)
                a.activation(hi.rearrange("p a b -> p (a b)"), wk[:, x0:x1], ACT.Copy).then_inc(w_hi, 1)
            n = 0
            for m, to in enumerate((dstT, srcT)):
                for b in range(4):
                    w = min(512, NG * GT - 512 * b)
                    act.wait_ge(et_made, n + 1)
                    a.activation(to[:, 512 * b:512 * b + w], ps[:, n % 2, 0:w], ACT.Copy).then_inc(et_read, 1)
                    n += 1
            for n in range(12):
                act.wait_ge(wt_made, n + 1)
                a.activation(Wg[0][:, :, n * P:(n + 1) * P], ps[:, 4 + n % 3, :].rearrange("p (k m) -> p k m", k=4), ACT.Copy).then_inc(wt_hi, 1)

            def gate(c, f, half, m, which):
                func = ACT.Tanh if which == 1 else ACT.Sigmoid
                col = (0, 2, 3)[which] * 4 + m
                return a.activation(sg[:, m % 2, which, :], ps[:, 4 + f % 3, half * CT:(half + 1) * CT], func,
                                    bias=gbias[:, col:col + 1]).then_inc(gate_act, 1)

            def chunk(c):
                act.wait_ge(trA, c + 1)
                a.activation(xa[0][:, 0:2, :], tr2[0], ACT.Copy).then_inc(xa_hi, 1)
                act.wait_ge(trX, c + 1)
                a.activation(xa[0][:, 2:4, :], tr2[1], ACT.Copy).then_inc(xa_hi, 1)
                for f in range(2):
                    act.wait_ge(fill_made, c * FILLS + f + 1)
                    for k in range(2):
                        m = 2 * f + k
                        x_ = a.activation(hf[:, m, :], ps[:, 4 + f, k * CT:(k + 1) * CT], ACT.Relu, bias=bias[:, m:m + 1]).then_inc(h_relu, 1)
                    act.wait_ge(h_relu, c * 4 + 2 * f + 2)
                    a.activation(hT[0][:, 2 * f:2 * f + 2, :], hf[:, 2 * f:2 * f + 2, :], ACT.Copy).then_inc(h_hi, 1)
                halves = [(0, 0), (0, 1), (0, 2), (1, 0), (1, 1), (1, 2), (2, 0), (2, 1), (2, 2), (3, 0), (3, 1), (3, 2)]

                def fill(f):
                    act.wait_ge(fill_made, c * FILLS + f + 1)
                    for k in range(2):
                        m, which = halves[2 * (f - 2) + k]
                        gate(c, f, k, m, which)

                def tanh_c(m):
                    act.wait_ge(c_made, c * 4 + m + 1)
                    a.activation(sg[:, m % 2, 1, :], sg[:, m % 2, 0, :], ACT.Tanh).then_inc(c_tanh, 1)

                def hi(m):
                    act.wait_ge(hl_made, c * 4 + m + 1)
                    a.activation(xa[0][:, m, :], hf[:, m, :], ACT.Copy).then_inc(hl_hi, 1)

                fill(2)
                fill(3)
                tanh_c(0)
                fill(4)
                hi(0)
                tanh_c(1)
                fill(5)
                hi(1)
                fill(6)
                tanh_c(2)
                fill(7)
                hi(2)
                tanh_c(3)
                hi(3)
                act.wait_ge(var_made, c + 1)
                a.activation(rstd, mv[:, :, 1], ACT.Sqrt, bias=epst[:, :]).then_inc(std_made, 1)
                act.wait_ge(x2T_made, c + 1)
                a.activation(x2nT, tr2[0], ACT.Copy).then_inc(x2T_copied, 1)

            act.wait_ge(bias_done, 2)
            with act.Fori(0, NCH) as c:
                chunk(c)

            def w_hi_parts(e, q):
                for n, (s, wb) in enumerate(((w1s, wbuf1[q]), (w2s, wbuf2[q]))):
                    act.wait_ge(stage_in, 32 * e + 32)
                    a.activation(wb[0], s, ACT.Copy).then_inc(stage_hi, 1)

            def half_work(e, h, q):
                hh = e * 2 + h
                nn = HALF[h]
                act.wait_ge(rows_in[h], 16 * e + 16)
                a.activation(es, rows[h][:, :, LOG:LOG + NEXP], ACT.Exp).then_inc(exp_made, 1)
                if h == 0:
                    a.activation(b1c[:, q, :], bias[:, ds(36 + e * 8, 8)], ACT.Copy).then_inc(b1_set, 1)
                act.wait_ge(rows_T, hh + 1)
                for k in range(2):
                    a.activation(xT[0][:, k, :], tr[k], ACT.Copy).then_inc(ex_hi, 1)
                for f in range(8):
                    act.wait_ge(mm1_made, hh * 8 + f + 1)
                    if f == 0:
                        act.wait_ge(b1_set, e + 1)
                    if f >= 2:
                        act.wait_ge(e_lo, hh * 8 + f - 1)
                    a.activation(hfE[:, f % 2, 0:nn], ps[:, 4 + f % 2, 0:nn], ACT.Relu,
                                 bias=b1c[:, q, f:f + 1]).then_inc(e_relu, 1)
                    act.wait_ge(e_relu, hh * 8 + f + 1)
                    if f >= 2:
                        act.wait_ge(h_used, hh * 6 + f - 1)
                    a.activation(hE[0][:, f % 2, 0:nn], hfE[:, f % 2, 0:nn], ACT.Copy).then_inc(e_hi, 1)

            act.wait_ge(experts_start, 1)
            w_hi_parts(0, 0)
            with act.Fori(0, NEXP // 2) as ep:
                for q in range(2):
                    e = ep * 2 + q
                    half_work(e, 0, q)
                    if q == 0:
                        w_hi_parts(e + 1, 1)
                    else:
                        with act.If(ep < NEXP // 2 - 1):
                            w_hi_parts(e + 1, 0)
                    half_work(e, 1, q)

        @block.vector
        def _(dve):
            v = nc.vector
            v.memset(ed[0][:, (TR - 1) * P:TR * P], PADDST).then_inc(pad_set, 1)
            v.memset(ed[1][:, (TR - 1) * P:TR * P], 0).then_inc(pad_set, 1)
            v.memset(epst[:, :], EPS).then_inc(start_marks, 1)
            v.memset(carry[:, :], 0.0).then_inc(carry_zero, 1)
            dve.wait_ge(edges_in, 6 * 16)
            for m in range(2):
                v.tensor_copy(edf[m], ed[m]).then_inc(edges_f, 1)
            dve.wait_ge(edges_f, 2)
            d3 = edf[0].rearrange("p (q e) -> p q e", q=TR)
            v.tensor_reduce(kmm[:, 0, :], d3, AX, ALU.min).then_inc(kmm_done, 1)
            v.tensor_reduce(kmm[:, 1, :], d3, AX, ALU.max).then_inc(kmm_done, 1)

            for i in range(7):
                nb = 8 if i < 6 else 1
                n = P if i < 6 else REST
                dve.wait_ge(x_in[i], 16)
                for b in range(nb):
                    v.bn_stats(ln_stats[0:n, b, :], agg[0:n, 8 * i + b, :]).then_inc(ln_chain, 1)
                dve.wait_ge(ln_chain, 8 * i + nb)
                for b in range(nb):
                    m_ = v.bn_aggr(ln_mv[0:n, b, :], ln_stats[0:n, b, :])
                m_.then_inc(ln_aggr, 1)
                dve.wait_ge(ln_sqrt, i + 1)
                v.reciprocal(ln_rstd[0:n, 0:nb], ln_rstd[0:n, 0:nb]).then_inc(ln_recip, 1)
                dve.wait_ge(ln_recip, i + 1)
                for b in range(nb):
                    v.tensor_scalar(agg[0:n, 8 * i + b, :], agg[0:n, 8 * i + b, :], ln_mv[0:n, b, 0:1], ln_rstd[0:n, b:b + 1],
                                    ALU.subtract, ALU.mult).then_inc(ln_done, 1)
                if i == 1:
                    for m, op in ((0, ALU.min), (1, ALU.max)):
                        dve.wait_ge(kmmT, 2)
                        v.tensor_reduce(gmm[0:TR, m, :], ps[0:TR, 7, m * P:(m + 1) * P].rearrange("p (g t) -> p g t", t=GT), AX, op).then_inc(g_reduced, 1)

            steps = [0]

            def link(ins):
                steps[0] += 1
                ins.then_inc(plan_chain, 1)
                dve.wait_ge(plan_chain, steps[0])

            dve.wait_ge(consts, 12)
            dve.wait_ge(g_back, 32)
            lo_r, hi_r = prow(0), prow(1)
            link(v.tensor_scalar(lo_r, lo_r, 7, None, ALU.arith_shift_right))
            link(v.tensor_scalar(hi_r, hi_r, 7, None, ALU.arith_shift_right))
            cnt = prow(2)
            link(v.scalar_tensor_tensor(cnt, hi_r, 1.0, lo_r, ALU.add, ALU.subtract))
            rdy = prow(1)
            link(v.tensor_copy(rdy, lo_r))
            s = 1
            while s < GPAD:
                link(v.tensor_tensor(prow(3, 0, GPAD - s), prow(1, 0, GPAD - s), prow(1, s, GPAD - s), ALU.min))
                link(v.tensor_copy(prow(1, 0, GPAD - s), prow(3, 0, GPAD - s)))
                s *= 2
            link(v.tensor_scalar(rdy, rdy, 1, None, ALU.arith_shift_right))
            link(v.scalar_tensor_tensor(rdy, rdy, float(NCH - 1), prow(4), ALU.min, ALU.subtract))
            link(v.tensor_scalar(rdy, rdy, 1.0, None, ALU.min))
            s = 1
            while s < GPAD:
                link(v.tensor_tensor(prow(3, 0, GPAD - s), prow(1, 0, GPAD - s), prow(1, s, GPAD - s), ALU.min))
                link(v.tensor_copy(prow(1, s, GPAD - s), prow(3, 0, GPAD - s)))
                s *= 2
            link(v.tensor_tensor(rdy, rdy, prow(4), ALU.add))
            flg = prow(3)
            link(v.tensor_copy(prow(3, 0, 1), prow(1, 0, 1)))
            link(v.tensor_tensor(prow(3, 1, GPAD - 1), prow(1, 1, GPAD - 1), prow(1, 0, GPAD - 1), ALU.subtract))
            link(v.scalar_tensor_tensor(cnt, cnt, 256.0, lo_r, ALU.mult, ALU.add))
            link(v.scalar_tensor_tensor(plan[:, :], flg, 65536.0, cnt, ALU.mult, ALU.add))

            for n in range(12):
                dve.wait_ge(wt_hi, n + 1)
                v.tensor_tensor(Wg[1][:, :, n * P:(n + 1) * P], ps[:, 4 + n % 3, :].rearrange("p (k m) -> p k m", k=4),
                                Wg[0][:, :, n * P:(n + 1) * P].bitcast(F32), ALU.subtract).then_inc(wt_lo, 1)
            dve.wait_ge(bias_T, 1)
            v.tensor_copy(bias[:, :], ps[:, 7, 256:356]).then_inc(bias_done, 1)
            dve.wait_ge(bias_done, 1)
            v.tensor_tensor(gbias[:, :], bias[:, 4:20], bias[:, 20:36], ALU.add).then_inc(bias_done, 1)
            dve.wait_ge(wt_made, 12)
            v.memset(wk[:, 4608:4608 + CH * ROW], 0.0).then_inc(zero_set, 1)
            dve.wait_ge(zero_set, 1)
            v.memset(sm[:, 0:1], 0.0).then_inc(pay_ready, 1)
            dve.wait_ge(consts, 12)
            v.tensor_scalar(valid[:, :], tok_code[:, :], float(N - NSLOT), None, ALU.is_lt).then_inc(start_marks, 1)
            dve.wait_ge(xn_out, 9 * 16)
            v.memset(agg[:, :, :], 0.0).then_inc(agg_zero, 1)
            dve.wait_ge(et_read, 8)
            v.memset(ps[:, 0, 0:D], 0.0).then_inc(S_used[0], 1)
            v.memset(ps[:, 1, 0:D], 0.0).then_inc(S_used[3], 1)
            v.memset(rel[:, 0:1], 0.0).then_inc(S_used[1], 1)
            v.memset(rel[:, 1:2], 0.0).then_inc(S_used[2], 1)
            v.memset(rel[:, 2:3], 0.0).then_inc(evac, 1)
            v.memset(rel[:, 3:4], 0.0).then_inc(S_made[GT - 1], 1)
            v.memset(sm[:, 2:3], 0.0).then_inc(x2_stored, 16)
            dve.wait_ge(agg_zero, 1)
            dve.wait_ge(S_used[1], 1)
            dve.wait_ge(S_used[2], 1)
            dve.wait_ge(evac, 1)
            dve.wait_ge(S_made[GT - 1], 1)
            dve.wait_ge(start_marks, 2)
            dve.wait_ge(small_in, 4 * 16)
            dve.wait_ge(plan_chain, steps[0])
            v.memset(sm[:, 3:4], 0.0).then_inc(plan_done, 1)

            vis = dve.alloc_register("dve_visit")
            prev = dve.alloc_register("dve_block_before")
            cc = dve.alloc_register("dve_chunk")
            mark = dve.alloc_register("dve_mark")
            r_lo, r_count, r_flag, r_n, r_b, r_bank = (dve.alloc_register("dve_" + k) for k in ("lo", "count", "flag", "n", "b", "bank"))
            for r in (vis, prev, cc):
                dve.reg_mov(r, 0)
            VMAX = NG * BLK

            def add_visit(n, b):
                dve.wait_ge(S_used[3], n + 1)
                dve.wait_ge(evac, n + 1)
                bank = held(dve, r_bank, (n + 1) & 1, 0, 1)
                v.tensor_tensor(agg[:, ds(b, 1), :], agg[:, ds(b, 1), :], ps[:, ds(bank, 1), 0:D], ALU.add).then_inc(evac, 1)

            def chunk(c, n_evac):
                K = [0]

                def step(ins):
                    K[0] += 1
                    ins.then_inc(route, 1)
                    dve.wait_ge(route, c * ROUTE + K[0])

                dve.wait_ge(evac, n_evac)
                v.tensor_copy(agg_blk, agg[:, ds(c * CH, CH), :]).then_inc(blk_copied, 1)
                dve.wait_ge(xr_in, 16 * c + 16)
                v.tensor_tensor(x_rows, x_rows, bfc[:, :, :].to_broadcast([P, CH, D]), ALU.add).then_inc(xb_made, 1)
                for k in range(2):
                    dve.wait_ge(xa_hi, c * 2 + k + 1)
                    v.tensor_tensor(xa[1][:, 2 * k:2 * k + 2, :], tr2[k], xa[0][:, 2 * k:2 * k + 2, :].bitcast(F32), ALU.subtract).then_inc(xa_lo, 1)
                for f in range(2):
                    dve.wait_ge(h_hi, c * 2 + f + 1)
                    v.tensor_tensor(hT[1][:, 2 * f:2 * f + 2, :], hf[:, 2 * f:2 * f + 2, :], hT[0][:, 2 * f:2 * f + 2, :].bitcast(F32), ALU.subtract).then_inc(h_lo, 1)

                def c_of(m):
                    dve.wait_ge(gate_act, c * 12 + 3 * m + 2)
                    v.tensor_tensor(sg[:, m % 2, 0, :], sg[:, m % 2, 0, :], sg[:, m % 2, 1, :], ALU.mult).then_inc(c_made, 1)

                def hl_of(m):
                    dve.wait_ge(c_tanh, c * 4 + m + 1)
                    dve.wait_ge(gate_act, c * 12 + 3 * m + 3)
                    v.tensor_tensor(hf[:, m, :], sg[:, m % 2, 1, :], sg[:, m % 2, 2, :], ALU.mult).then_inc(hl_made, 1)

                def lo_of(m):
                    dve.wait_ge(hl_hi, c * 4 + m + 1)
                    v.tensor_tensor(xa[1][:, m, :], hf[:, m, :], xa[0][:, m, :].bitcast(F32), ALU.subtract).then_inc(hl_lo, 1)

                c_of(0)
                hl_of(0)
                c_of(1)
                lo_of(0)
                hl_of(1)
                c_of(2)
                lo_of(1)
                hl_of(2)
                c_of(3)
                lo_of(2)
                hl_of(3)
                lo_of(3)
                dve.wait_ge(scattered, 16 * CH * (c + 1))
                dve.wait_ge(x2_stored, 16 * c + 16)
                dve.wait_ge(fill_made, c * FILLS + 9)
                dve.wait_ge(xb_made, c + 1)
                v.tensor_tensor(pay[:, :, RES:RES + D], ps[:, 6, :].rearrange("p (b d) -> p b d", b=CH), x_rows, ALU.add).then_inc(x2_made, 1)
                dve.wait_ge(x2_made, c + 1)
                for b in range(CH):
                    i_ = v.bn_stats(stats[:, b, :], pay[:, b, RES:RES + D])
                step(i_)
                i_ = v.tensor_copy(pay[:, :, TOK:TOK + 1].rearrange("p b o -> p (b o)"), tok_code[:, ds(c * CH, CH)])
                for b in range(CH):
                    i_ = v.bn_aggr(mv[:, b, :], stats[:, b, :])
                i_.then_inc(var_made, 1)
                dve.wait_ge(std_made, c + 1)
                step(v.reciprocal(rstd, rstd))
                for b in range(CH):
                    v.tensor_scalar(pay[:, b, 0:D], pay[:, b, RES:RES + D], mv[:, b, 0:1], rstd[:, b:b + 1],
                                    ALU.subtract, ALU.mult).then_inc(x2n_made, 1)
                dve.wait_ge(logit_made, c + 1)
                step(v.tensor_tensor(lg, tr[1][:, 0:CH * NEXP].rearrange("p (b e) -> p b e", b=CH), gb[:, :, :], ALU.add))
                step(v.tensor_reduce(mx, lg, AX, ALU.max))
                for b in range(CH):
                    i_ = v.tensor_scalar(pay[:, b, LOG:LOG + NEXP], lg[:, b, :], mx[:, b:b + 1], None, ALU.subtract)
                step(i_)
                step(v.scalar_tensor_tensor(sc, pay[:, :, LOG:LOG + NEXP], 0.0, e_rank[:, :, :], ALU.is_ge, ALU.mult))
                step(v.tensor_reduce(m2, sc, AX, ALU.max))
                for b in range(CH):
                    i_ = v.tensor_scalar(oh[:, b, :], sc[:, b, :], m2[:, b:b + 1], valid[:, ds(c * CH + b, 1)], ALU.is_equal, ALU.mult)
                step(i_)
                dve.wait_ge(cum_made, c + 1)
                step(v.tensor_tensor(pin, tr[1][:, 32:32 + CH * NEXP].rearrange("p (b e) -> p b e", b=CH),
                                     carry[:, :].rearrange("p (o e) -> p o e", o=1).to_broadcast([P, CH, NEXP]), ALU.add))
                v.tensor_tensor(pp, pin, oh[:, :, :], ALU.mult)
                step(v.tensor_tensor(pw, pin, e_base[:, :, :], ALU.add))
                step(v.tensor_tensor(pw, pw, oh[:, :, :], ALU.mult))
                v.tensor_reduce(psum_, pp, AX, ALU.add)
                v.tensor_tensor(carry[:, :], carry[:, :], tr[1][:, 48:48 + NEXP], ALU.add)
                step(v.tensor_reduce(wsum, pw, AX, ALU.add))
                step(v.tensor_scalar(kept, psum_, float(CAP), None, ALU.is_le))
                step(v.scalar_tensor_tensor(kept2, psum_, 1.0, kept, ALU.is_ge, ALU.mult))
                step(v.scalar_tensor_tensor(slotf, wsum, float(-1 - NOSLOT), kept2, ALU.add, ALU.mult))
                dve.wait_ge(pay_ready, c + 1)
                v.tensor_scalar(idx[:, :], slotf, float(NOSLOT), None, ALU.add).then_inc(pay_ready, 1)
                assert K[0] == ROUTE, K

            with dve.Fori(0, NG) as gq:
                dve.load(mark, plan[0:1, ds(gq, 1)])
                word = dve.snap(mark, min_val=0, max_val=(1 << 17) - 1)
                lo = held(dve, r_lo, word & 255, 0, BLK - 1)
                count = held(dve, r_count, (word >> 8) & 255, 1, BLK)
                flag = held(dve, r_flag, word >> 16, 0, 1)
                n0 = dve.snap(vis, min_val=0, max_val=VMAX - BLK)
                with dve.Fori(0, count) as j:
                    n = held(dve, r_n, n0 + j, 0, VMAX)
                    b = held(dve, r_b, lo + j, 0, BLK - 1)
                    dve.wait_ge(S_made[GT - 1], n + 1)
                    v.tensor_scalar(rel[:, :], dstT[:, ds(gq * GT, GT)], blk_base[:, ds(b, 1)], None, ALU.subtract).then_inc(rel_made, 1)
                    dve.wait_ge(rel_made, n + 1)
                    for t in range(GT):
                        dve.wait_ge(S_used[t], n + 1)
                        v.tensor_scalar(S[:, t, :], iota_d[:, :], rel[:, t:t + 1], None, ALU.is_equal).then_inc(S_made[t], 1)
                    before = dve.snap(prev, min_val=0, max_val=BLK - 1)
                    add_visit(n, before)
                    dve.reg_mov(prev, b)
                dve.reg_mov(vis, n0 + count)
                with dve.If(flag > 0):
                    c = dve.snap(cc, min_val=0, max_val=NCH - 1)
                    nv = dve.snap(vis, min_val=1, max_val=VMAX)
                    chunk(c, nv + 1)
                    dve.reg_mov(cc, c + 1)
            nv = dve.snap(vis, min_val=1, max_val=VMAX)
            before = dve.snap(prev, min_val=0, max_val=BLK - 1)
            add_visit(nv, before)
            c0 = dve.snap(cc, min_val=0, max_val=NCH - 1)
            with dve.Fori(c0, NCH) as c:
                chunk(c, nv + 2)

            v.memset(sm[:, 3:4], 0.0).then_inc(stage_lo, 1)
            v.memset(sm[:, 4:5], 0.0).then_inc(o_made, O_INIT)
            v.memset(sm[:, 5:6], 0.0).then_inc(y_read, Y_INIT)
            v.memset(sm[:, 6:7], 0.0).then_inc(q_made, 1)
            v.memset(sm[:, 7:8], 0.0).then_inc(r_made, 1)
            v.memset(tok_i[:, :], NOSLOT).then_inc(tok_made, 1)
            v.memset(sm[:, 8:9], 0.0).then_inc(experts_start, 1)

            def half_work(e, h, q):
                hh = e * 2 + h
                nn = HALF[h]
                dve.wait_ge(rows_in[h], 16 * e + 16)
                dve.wait_ge(exp_made, hh + 1)
                v.tensor_reduce(ssum, es, AX, ALU.add).then_inc(weight_chain, 1)
                v.tensor_scalar(tokf, rows[h][:, :, TOK:TOK + 1].rearrange("p t o -> p (t o)"), float(NSLOT), None, ALU.add).then_inc(weight_chain, 1)
                dve.wait_ge(weight_chain, hh * 3 + 2)
                v.reciprocal(rp, ssum).then_inc(weight_chain, 1)
                for k in range(2):
                    dve.wait_ge(ex_hi, hh * 2 + k + 1)
                    v.tensor_tensor(xT[1][:, k, :], tr[k], xT[0][:, k, :].bitcast(F32), ALU.subtract).then_inc(ex_lo, 1)
                for f in range(8):
                    dve.wait_ge(e_hi, hh * 8 + f + 1)
                    v.tensor_tensor(hE[1][:, f % 2, 0:nn], hfE[:, f % 2, 0:nn], hE[0][:, f % 2, 0:nn].bitcast(F32), ALU.subtract).then_inc(e_lo, 1)
                dve.wait_ge(b2_in, 16 * e + 16)
                for u in range(2):
                    un = hh * 2 + u
                    dve.wait_ge(q_made, un + 1)
                    dve.wait_ge(y_made, un + 1)
                    bank = 0 if u == 0 else 6
                    v.tensor_tensor(yb, ps[:, bank:bank + 2, 0:D], b2t[q].rearrange("p (o d) -> p o d", o=1).to_broadcast([P, 2, D]),
                                    ALU.add).then_inc(y_read, 1)
                    dve.wait_ge(y_read, Y_INIT + un + 1)
                    dve.wait_ge(weight_chain, hh * 3 + 3)
                    for t in range(2):
                        i_ = v.tensor_scalar(qv[u][:, t, :], yb[:, t, :], rp[:, 2 * u + t:2 * u + t + 1], None, ALU.mult)
                    i_.then_inc(q_made, 1)
                for u in range(2):
                    un = hh * 2 + u
                    dve.wait_ge(q_made, un + 2)
                    v.tensor_scalar(fin_mask[:, :, :], qv[u], 0.0, 0.0, ALU.mult, ALU.is_equal).then_inc(out_chain, 1)
                    dve.wait_ge(out_chain, un * 2 + 1)
                    dve.wait_ge(r_made, un + 2)
                    dve.wait_ge(out_scattered[u], 32 * hh + 32)
                    v.tensor_copy(tok_i[:, 2 * u:2 * u + 2], tokf[:, 2 * u:2 * u + 2]).then_inc(tok_made, 1)
                    v.copy_predicated(rr[u], fin_mask[:, :, :], qv[u]).then_inc(out_chain, 1)
                    dve.wait_ge(out_chain, un * 2 + 2)
                    v.tensor_tensor(ov[u], rr[u], rows[h][:, 2 * u:2 * u + 2, RES:RES + D], ALU.add).then_inc(o_made, 1)

            with dve.Fori(0, NEXP // 2) as ep:
                for q in range(2):
                    for h in range(2):
                        half_work(ep * 2 + q, h, q)

        @block.tensor
        def _(pe):
            t_ = nc.tensor
            pe.wait_ge(consts, 12)
            pe.wait_ge(kmm_done, 2)
            for m in range(2):
                t_.transpose(ps[0:TR, 7, m * P:(m + 1) * P], kmm[:, m, :], ident[:, :]).then_inc(kmmT, 1)
            n = 0
            for m in range(2):
                for b in range(4):
                    if n >= 2:
                        pe.wait_ge(et_read, n - 1)
                    for k in range(4 if b < 3 else 1):
                        i_ = t_.transpose(ps[:, n % 2, k * P:(k + 1) * P], edf[m][:, (4 * b + k) * P:(4 * b + k + 1) * P], ident[:, :])
                    i_.then_inc(et_made, 1)
                    n += 1
            pe.wait_ge(g_reduced, 2)
            pe.wait_ge(bias_in, 64)
            t_.transpose(ps[:, 7, 256:356], b_stage[0:100, :], ident[0:100, 0:100]).then_inc(bias_T, 1)
            for n in range(12):
                q, r = n // 4, n % 4
                pe.wait_ge((w_in, w_in2, w_in3)[q], (64, 16, 16)[q])
                if n >= 3:
                    pe.wait_ge(wt_lo, n - 2)
                st = cut(wk, 0 if q == 1 else 3072, 4, H)
                for k in range(4):
                    i_ = t_.transpose(ps[:, 4 + n % 3, k * P:(k + 1) * P], st[:, r, k * P:(k + 1) * P], ident[:, :])
                i_.then_inc(wt_made, 1)

            def split3(o, w, xx, wsel, xsel, first, last, swap=False):
                for n, (p, q) in enumerate(((0, 0), (0, 1), (1, 0))):
                    i_ = t_.matmul(o, wsel(w[p]), xsel(xx[q]), start=first and n == 0, stop=last and n == 2)
                return i_

            pe.wait_ge(wt_lo, 12)
            pe.wait_ge(w_lo, 3)
            vis = pe.alloc_register("pe_visit")
            cc = pe.alloc_register("pe_chunk")
            mark = pe.alloc_register("pe_mark")
            r_count, r_flag, r_slot, r_n, r_bank = (pe.alloc_register("pe_" + k) for k in ("count", "flag", "slot", "n", "bank"))
            for r in (vis, cc):
                pe.reg_mov(r, 0)
            VMAX = NG * BLK

            def chunk(c):
                pe.wait_ge(blk_copied, c + 1)
                for b in range(CH):
                    for k in range(2):
                        i_ = t_.transpose(tr2[0][:, k, b * P:(b + 1) * P], agg_blk[:, b, k * P:(k + 1) * P], ident[:, :])
                i_.then_inc(trA, 1)
                pe.wait_ge(xn_in, 16 * c + 16)
                for b in range(CH):
                    for k in range(2):
                        i_ = t_.transpose(tr2[1][:, k, b * P:(b + 1) * P], xn_rows[:, b, k * P:(k + 1) * P], ident[:, :])
                i_.then_inc(trX, 1)
                for f in range(2):
                    for k2 in range(2):
                        m = 2 * f + k2
                        for k in range(4):
                            if f == 0 and k2 == 0 and k % 2 == 0:
                                pe.wait_ge(xa_lo, c * 2 + k // 2 + 1)
                            i_ = split3(ps[:, 4 + f, k2 * CT:(k2 + 1) * CT], Wrr, xa,
                                        lambda w: w[:, k, m * P:(m + 1) * P], lambda y: y[:, k, :], k == 0, k == 3)
                    i_.then_inc(fill_made, 1)
                halves = [(m, w) for m in range(4) for w in range(3)]
                for f in range(2, 8):
                    if f < 5:
                        if f < 4:
                            if f == 3:
                                pe.wait_ge(h_relu, c * 4 + 2)
                        else:
                            pe.wait_ge(h_relu, c * 4 + 4)
                    else:
                        pe.wait_ge(gate_act, c * 12 + 2 * (f - 4))
                    for k2 in range(2):
                        m, w_ = halves[2 * (f - 2) + k2]
                        for k in range(4):
                            if f == 2 and k2 == 0 and k % 2 == 0:
                                pe.wait_ge(h_lo, c * 2 + k // 2 + 1)
                            col = w_ * H + m * P
                            i_ = split3(ps[:, 4 + f % 3, k2 * CT:(k2 + 1) * CT], Wg, hT,
                                        lambda w: w[:, k, col:col + P], lambda y: y[:, k, :], k == 0, k == 3)
                    i_.then_inc(fill_made, 1)
                pe.wait_ge(gate_act, c * 12 + 8)
                for b in range(CH):
                    for k in range(4):
                        if b == 0:
                            pe.wait_ge(hl_lo, c * 4 + k + 1)
                        for n, (p, q) in enumerate(((0, 0), (0, 1), (1, 0))):
                            i_ = t_.matmul(ps[:, 6, b * D:(b + 1) * D], xa[p][:, k, b * P:(b + 1) * P], Wfc[q][:, k, :],
                                           start=(k == 0 and n == 0), stop=(k == 3 and n == 2))
                i_.then_inc(fill_made, 1)
                pe.wait_ge(x2n_made, c * CH + CH)
                for b in range(CH):
                    for k in range(2):
                        i_ = t_.transpose(tr2[0][:, k, b * P:(b + 1) * P], pay[:, b, k * P:(k + 1) * P], ident[:, :])
                i_.then_inc(x2T_made, 1)
                pe.wait_ge(x2T_copied, c + 1)
                for b in range(CH):
                    for k in range(2):
                        i_ = t_.matmul(tr[1][:, b * NEXP:(b + 1) * NEXP], x2nT[:, k, b * P:(b + 1) * P], gw[:, k, :],
                                       start=(k == 0), stop=(k == 1))
                i_.then_inc(logit_made, 1)
                pe.wait_ge(route, c * ROUTE + 8)
                for b in range(CH):
                    t_.matmul(tr[1][:, 32 + b * NEXP:32 + (b + 1) * NEXP], tri[:, :], oh[:, b, :], start=True, stop=(b == 0))
                    for b0 in range(b):
                        t_.matmul(tr[1][:, 32 + b * NEXP:32 + (b + 1) * NEXP], ones[:, :], oh[:, b0, :], start=False, stop=(b0 == b - 1))
                for b in range(CH):
                    i_ = t_.matmul(tr[1][:, 48:48 + NEXP], ones[:, :], oh[:, b, :], start=(b == 0), stop=(b == CH - 1))
                i_.then_inc(cum_made, 1)

            pe.wait_ge(plan_done, 1)
            pe.wait_ge(bias_done, 1)
            with pe.Fori(0, NG) as gq:
                pe.load(mark, plan[0:1, ds(gq, 1)])
                word = pe.snap(mark, min_val=0, max_val=(1 << 17) - 1)
                count = held(pe, r_count, (word >> 8) & 255, 1, BLK)
                flag = held(pe, r_flag, word >> 16, 0, 1)
                slot = held(pe, r_slot, gq & (RING - 1), 0, RING - 1)
                n0 = pe.snap(vis, min_val=0, max_val=VMAX - BLK)
                with pe.Fori(0, count) as j:
                    pe.wait_ge(ring_ready, gq + 1)
                    n = held(pe, r_n, n0 + j, 0, VMAX)
                    bank = held(pe, r_bank, n & 1, 0, 1)
                    pe.wait_ge(evac, n + 1)
                    for t in range(GT):
                        pe.wait_ge(S_made[t], n + (2 if t == GT - 1 else 1))
                        t_.matmul(ps[:, ds(bank, 1), 0:D], S[:, t, :], ring[:, ds(slot, 1), t, :],
                                  start=(t == 0), stop=(t == GT - 1)).then_inc(S_used[t], 1)
                pe.reg_mov(vis, n0 + count)
                t_.matmul(ps[:, 7, 0:4], ones[:, :], ones[:, 0:4], start=True, stop=True).then_inc(group_done, 1)
                with pe.If(flag > 0):
                    c = pe.snap(cc, min_val=0, max_val=NCH - 1)
                    chunk(c)
                    pe.reg_mov(cc, c + 1)
            c0 = pe.snap(cc, min_val=0, max_val=NCH - 1)
            with pe.Fori(c0, NCH) as c:
                chunk(c)

            def mm1(hh, h, q, f):
                nn = HALF[h]
                w = [wbuf1[q][p].rearrange("p (k n) -> p k n", k=2) for p in range(2)]
                for k in range(2):
                    if f == 0:
                        pe.wait_ge(ex_lo, hh * 2 + k + 1)
                    i_ = split3(ps[:, 4 + f % 2, 0:nn], w, xT, lambda y: y[:, k, f * P:(f + 1) * P], lambda y: y[:, k, 0:nn], k == 0, k == 1)
                i_.then_inc(mm1_made, 1)

            def mm2(hh, h, q, f):
                w = [wbuf2[q][p].rearrange("p (k n) -> p k n", k=8) for p in range(2)]
                pe.wait_ge(e_lo, hh * 8 + f + 1)
                banks = (0, 1, 6, 7)
                for t in range(4):
                    if f == 0 and t % 2 == 0:
                        pe.wait_ge(y_read, Y_INIT + hh * 2 + t // 2 - 1)
                    for n, (p, r) in enumerate(((0, 0), (0, 1), (1, 0))):
                        i_ = t_.matmul(ps[:, banks[t], 0:D], hE[p][:, f % 2, t * P:(t + 1) * P], w[r][:, f, :],
                                       start=(f == 0 and n == 0), stop=(f == 7 and n == 2))
                    if f == 7 and t % 2 == 1:
                        i_.then_inc(y_made, 1)
                if f < 6:
                    i_.then_inc(h_used, 1)

            pe.wait_ge(experts_start, 1)
            with pe.Fori(0, NEXP // 2) as ep:
                for q in range(2):
                    e = ep * 2 + q
                    pe.wait_ge(stage_lo, e * 2 + 2 + 1)
                    for h in range(2):
                        hh = e * 2 + h
                        pe.wait_ge(rows_in[h], 16 * e + 16)
                        for k in range(2):
                            for t in range(4):
                                i_ = t_.transpose(tr[k][:, t * P:(t + 1) * P], rows[h][:, t, k * P:(k + 1) * P], ident[:, :])
                        i_.then_inc(rows_T, 1)
                        for f in range(8):
                            mm1(hh, h, q, f)
                            if f:
                                mm2(hh, h, q, f - 1)
                        mm2(hh, h, q, 7)


_PRE = ["x", "src", "dst"]
_GNN = ["W_rel", "b_rel", "W_root", "W_ih", "W_hh", "b_ih", "b_hh", "W_fc", "b_fc"]
_FFN = ["gate_w", "gate_b", "w1", "b1", "w2", "b2"]
_INS = _PRE + ["L0_gnn_" + n for n in _GNN] + ["L0_ffn_" + n for n in _FFN]


def kernel(**inputs):
    import numpy as _np
    import concourse.bacc as _bacc
    from concourse import mybir as _mybir
    from concourse.bass_utils import run_bass_kernel_spmd as _run

    nc = _bacc.Bacc("TRN2", target_bir_lowering=False, num_devices=1)
    arrays, args = {}, []
    for name in _INS:
        a = _np.ascontiguousarray(inputs[name])
        arrays[f"in_{name}_dram"] = a
        args.append(nc.dram_tensor(f"in_{name}_dram", a.shape, _mybir.dt.from_np(a.dtype), kind="ExternalInput").ap())
    args.append(nc.dram_tensor("out_0_dram", (N, D), _mybir.dt.float32, kind="ExternalOutput").ap())
    build(nc, *args)
    r = _run(nc, [arrays], core_ids=[0])
    return r.results[0]["out_0_dram"]
```
